# Optimizing a Trainium2 kernel written in Bass

```python
import numpy as np
import jax
import jax.numpy as jnp

def _softmax(x, axis=-1):
    return jax.nn.softmax(x, axis=axis)

def _gelu(x):
    return jax.nn.gelu(x, approximate=True)

def _silu(x):
    return jax.nn.silu(x)

def _sigmoid(x):
    return jax.nn.sigmoid(x)

def _layernorm(x, axis=-1, eps=1e-05):
    m = jnp.mean(x, axis=axis, keepdims=True)
    v = jnp.var(x, axis=axis, keepdims=True)
    return (x - m) / jnp.sqrt(v + eps)

def _scatter_add(tgt, idx, src, axis=0):
    return tgt.at[idx].add(src)

def _segment_sum(src, seg, n):
    return jax.ops.segment_sum(src, seg, n)
kernel_name = 'mk_gnn_preln_d2_gnn_r8_708ed3'

def setup_inputs(seed: int=0):
    np.random.seed(seed)
    _w = jnp.asarray

    def _rec_inputs():
        import jax
        import jax.numpy as jnp
        _gk = jax.random.key(seed)
        x = -0.000202 + 1 * jax.random.normal(jax.random.fold_in(_gk, 1), (12500, 64), jnp.float32)
        src = jax.random.randint(jax.random.fold_in(_gk, 2), (200000,), 0, 12500, jnp.int32)
        dst = jax.random.randint(jax.random.fold_in(_gk, 3), (200000,), 0, 12500, jnp.int32)
        _o = jnp.argsort(dst, stable=True)
        src = src[_o]
        dst = dst[_o]
        edge_attr_64 = -8.16379e-05 + 0.999858 * jax.random.normal(jax.random.fold_in(_gk, 11), (200000, 64), jnp.float32)
        return (x, src, dst, edge_attr_64)
    x, src, dst, edge_attr_64 = _rec_inputs()

    def _L0_gnn_setup():
        import jax, jax.numpy as jnp
        import numpy as np
        N_NODES = 12500

        def sage_conv(x, src, dst, w_self, w_nei, b):
            agg = jax.ops.segment_sum(x[src], dst, num_segments=N_NODES)
            deg = jax.ops.segment_sum(jnp.ones((src.shape[0], 1), x.dtype), dst, num_segments=N_NODES)
            mean = agg / jnp.maximum(deg, 1.0)
            return x @ w_self + mean @ w_nei + b
        key = jax.random.key(seed)
        ks = jax.random.split(key, 12)
        d_in, d_hid, d_out = (64, 64, 64)
        E = 200000
        s = lambda d: 1.0 / np.sqrt(d)
        return {'x': jax.random.normal(ks[0], (N_NODES, d_in), jnp.float32), 'edge_index': jax.random.randint(ks[1], (2, E), 0, N_NODES, jnp.int64), 'w_self1': jax.random.normal(ks[2], (d_in, d_hid), jnp.float32) * s(d_in), 'w_nei1': jax.random.normal(ks[3], (d_in, d_hid), jnp.float32) * s(d_in), 'b1': jnp.zeros((d_hid,), jnp.float32), 'w_self2': jax.random.normal(ks[4], (d_hid, d_hid), jnp.float32) * s(d_hid), 'w_nei2': jax.random.normal(ks[5], (d_hid, d_hid), jnp.float32) * s(d_hid), 'b2': jnp.zeros((d_hid,), jnp.float32), 'w_self3': jax.random.normal(ks[6], (d_hid, d_out), jnp.float32) * s(d_hid), 'w_nei3': jax.random.normal(ks[7], (d_hid, d_out), jnp.float32) * s(d_hid), 'b3': jnp.zeros((d_out,), jnp.float32)}
    _L0_gnn_all = _L0_gnn_setup()
    _L0_gnn_in = {k: v for k, v in _L0_gnn_all.items() if k in ('w_self1', 'w_nei1', 'b1', 'w_self2', 'w_nei2', 'b2', 'w_self3', 'w_nei3', 'b3')}
    del _L0_gnn_all

    def _L1_gnn_setup():
        import jax, jax.numpy as jnp
        import numpy as np
        N = 12500
        E = 200000
        D = 64
        key = jax.random.key(seed)
        ks = jax.random.split(key, 6)
        scale = 1.0 / np.sqrt(3 * D)
        return {'h_e': jax.random.normal(ks[0], (N, D), dtype=jnp.float32), 'h_r': jax.random.normal(ks[1], (E, D), dtype=jnp.float32), 'W1': jax.random.normal(ks[2], (3 * D, D), dtype=jnp.float32) * scale, 'b1': jnp.zeros((D,), dtype=jnp.float32), 'W2': jax.random.normal(ks[3], (3 * D, D), dtype=jnp.float32) * scale, 'b2': jnp.zeros((D,), dtype=jnp.float32), 'edge_index': jax.random.randint(ks[4], (2, E), 0, N, dtype=jnp.int64)}
    _L1_gnn_all = _L1_gnn_setup()
    _L1_gnn_in = {k: v for k, v in _L1_gnn_all.items() if k in ('W1', 'b1', 'W2', 'b2')}
    del _L1_gnn_all
    return {'x': x, 'src': src, 'dst': dst, 'edge_attr_64': edge_attr_64, 'L0_gnn_w_self1': _L0_gnn_in['w_self1'], 'L0_gnn_w_nei1': _L0_gnn_in['w_nei1'], 'L0_gnn_b1': _L0_gnn_in['b1'], 'L0_gnn_w_self2': _L0_gnn_in['w_self2'], 'L0_gnn_w_nei2': _L0_gnn_in['w_nei2'], 'L0_gnn_b2': _L0_gnn_in['b2'], 'L0_gnn_w_self3': _L0_gnn_in['w_self3'], 'L0_gnn_w_nei3': _L0_gnn_in['w_nei3'], 'L0_gnn_b3': _L0_gnn_in['b3'], 'L1_gnn_W1': _L1_gnn_in['W1'], 'L1_gnn_b1': _L1_gnn_in['b1'], 'L1_gnn_W2': _L1_gnn_in['W2'], 'L1_gnn_b2': _L1_gnn_in['b2']}

def reference(x, src, dst, edge_attr_64, L0_gnn_w_self1, L0_gnn_w_nei1, L0_gnn_b1, L0_gnn_w_self2, L0_gnn_w_nei2, L0_gnn_b2, L0_gnn_w_self3, L0_gnn_w_nei3, L0_gnn_b3, L1_gnn_W1, L1_gnn_b1, L1_gnn_W2, L1_gnn_b2):
    import jax
    import jax.numpy as jnp

    def _L0_gnn_ref(x, edge_index, w_self1, w_nei1, b1, w_self2, w_nei2, b2, w_self3, w_nei3, b3):
        import jax, jax.numpy as jnp
        import numpy as np
        N_NODES = 12500

        def sage_conv(x, src, dst, w_self, w_nei, b):
            agg = jax.ops.segment_sum(x[src], dst, num_segments=N_NODES)
            deg = jax.ops.segment_sum(jnp.ones((src.shape[0], 1), x.dtype), dst, num_segments=N_NODES)
            mean = agg / jnp.maximum(deg, 1.0)
            return x @ w_self + mean @ w_nei + b
        src, dst = (edge_index[0], edge_index[1])
        h = jax.nn.relu(sage_conv(x, src, dst, w_self1, w_nei1, b1))
        h = jax.nn.relu(sage_conv(h, src, dst, w_self2, w_nei2, b2))
        h = sage_conv(h, src, dst, w_self3, w_nei3, b3)
        return h

    def _L1_gnn_ref(h_e, h_r, W1, b1, W2, b2, edge_index):
        import jax, jax.numpy as jnp
        import numpy as np
        N = 12500
        E = 200000
        D = 64
        src = edge_index[0]
        dst = edge_index[1]
        n = h_e.shape[0]
        deg = jax.ops.segment_sum(jnp.ones((src.shape[0],), h_e.dtype), dst, num_segments=n)
        inv_deg = (1.0 / jnp.maximum(deg, 1.0))[:, None]
        nbr_r = jax.ops.segment_sum(h_r, dst, num_segments=n) * inv_deg

        def layer(h, W, b):
            nbr_x = jax.ops.segment_sum(h[src], dst, num_segments=n) * inv_deg
            z = jnp.concatenate([h, nbr_x, nbr_r], axis=1)
            return jax.nn.relu(z @ W + b)
        h = layer(h_e, W1, b1)
        h = layer(h, W2, b2)
        return h
    edge_index = jnp.stack([src, dst])
    h = jnp.maximum(_layernorm(x, axis=-1), 0.0)
    x = x + _L0_gnn_ref(h, edge_index, L0_gnn_w_self1, L0_gnn_w_nei1, L0_gnn_b1, L0_gnn_w_self2, L0_gnn_w_nei2, L0_gnn_b2, L0_gnn_w_self3, L0_gnn_w_nei3, L0_gnn_b3)
    h = jnp.maximum(_layernorm(x, axis=-1), 0.0)
    x = x + _L1_gnn_ref(h, edge_attr_64, L1_gnn_W1, L1_gnn_b1, L1_gnn_W2, L1_gnn_b2, edge_index)
    return x

_drawn_inputs = setup_inputs


def setup_inputs(seed=0):
    import zlib

    import numpy as np

    out = dict(_drawn_inputs(seed))
    spreads = {'L0_gnn_b1': (0.0, 0.1),
     'L0_gnn_b2': (0.0, 0.1),
     'L0_gnn_b3': (0.0, 0.1),
     'L1_gnn_b1': (0.0, 0.32),
     'L1_gnn_b2': (0.0, 0.1)}
    factors = {}
    for name, (base, spread) in spreads.items():
        noise = np.random.default_rng([zlib.crc32(name.encode()), seed]).standard_normal(out[name].shape)
        drawn = base * np.exp(spread * noise) if base else spread * noise
        out[name] = jnp.asarray(drawn.astype(out[name].dtype))
    for name, factor in factors.items():
        out[name] = (out[name] * factor).astype(out[name].dtype)
    return out
```

```python
from contextlib import ExitStack

import concourse.bass as bass
from concourse import mybir

F32 = mybir.dt.float32
I32 = mybir.dt.int32
U32 = mybir.dt.uint32
ALU = mybir.AluOpType
ACT = mybir.ActivationFunctionType
AX_X = mybir.AxisListType.X

P = 128
N = 12500
E = 200000
D = 64
EPS = 1e-05
NODES_PP = -(-N // P)
NPAD = P * NODES_PP
TILES = 4
UNIT = P * TILES
WIN = 64
UPG = 2
TPG = UPG * TILES
GROUPS = 196
UNITS = GROUPS * UPG
RING = 4
ITERS = GROUPS // RING
ZPIECE = -(-(N + WIN) // ITERS)
ZW = ITERS * ZPIECE
assert ZW >= NPAD and GROUPS % RING == 0 and UNITS * UNIT >= E
CH = 7
BODY = 2 * CH
BODIES = NODES_PP // BODY
CHUNKS = 2 * BODIES
TCOLS = CH * D
LAYERS = 5
FULL_BLOCKS = E // (P * UNIT)
TAIL_UNITS = UNITS - FULL_BLOCKS * P
TAIL_FULL = (E - FULL_BLOCKS * P * UNIT) // UNIT
TAIL_REST = E - (FULL_BLOCKS * P + TAIL_FULL) * UNIT
LAST_P = P - 1
LAST_NODES = N - LAST_P * NODES_PP
XSPLIT = 112
SUMS_CREDIT = 4


class Steps:

    def __init__(self, eng, sem):
        self.eng, self.sem, self.base, self.per, self.index, self.n = eng, sem, 0, 0, None, 0

    def enter(self, per, index):
        self.per, self.index, self.n = per, index, 0

    def leave(self, trips):
        self.base += self.per * trips
        self.per, self.index, self.n = 0, None, 0

    def done(self, ins):
        ins.then_inc(self.sem, 1)
        if self.index is None:
            self.base += 1
            self.eng.wait_ge(self.sem, self.base)
        else:
            self.n += 1
            self.eng.wait_ge(self.sem, self.base + self.per * self.index + self.n)


def program(nc, a, out):
    with ExitStack() as ctx:
        def sb(name, shape, dt=F32):
            return ctx.enter_context(nc.sbuf_tensor(name, shape, dt))

        def psum(name, shape):
            return ctx.enter_context(nc.psum_tensor(name, shape, F32))

        def sem(name):
            return ctx.enter_context(nc.semaphore(name))

        table = [nc.dram_tensor(f"table{i}", (NPAD, D), F32).ap() for i in range(2)]
        x1_dram = nc.dram_tensor("x1_rows", (NPAD, D), F32).ap()

        z = [sb(f"z{i}", [P, ZW]) for i in range(2)]
        rd = sb("rd", [P, ZW])
        src_t = sb("src_t", [P, UNITS * TILES])
        dst_t = sb("dst_t", [P, UNITS * TILES])
        msg = sb("msg", [P, RING, TPG, 2 * D])
        idx = sb("idx", [P, RING, TPG], U32)
        onehot = sb("onehot", [P, 2, TPG, WIN])
        xin = sb("xin", [P, BODY, D])
        cent = sb("cent", [P, BODY, D])
        vbuf = sb("vbuf", [P, BODY, D])
        hbuf = sb("hbuf", [P, 2, CH, D])
        mean = sb("mean", [P, BODY])
        var = sb("var", [P, BODY])
        std = sb("std", [P, BODY])
        eps = sb("eps", [P, 1])
        ident = sb("ident", [P, P])
        ones = sb("ones", [P, P])
        diag = sb("diag", [P, P])
        iota = sb("iota", [P, WIN])
        iota_r = sb("iota_r", [P, WIN])
        shift = sb("shift", [P, 1])
        zeros = sb("zeros", [P, ZPIECE])
        wcat = sb("wcat", [P, LAYERS, D])
        wr = sb("wr", [P, 2, D])
        bias_bc = sb("bias_bc", [P, LAYERS, D])
        bias_col = sb("bias_col", [D, LAYERS])
        dlow = sb("dlow", [P, 4])
        dhigh = sb("dhigh", [P, 4])
        dspan = sb("dspan", [P, 4])
        pspan = sb("pspan", [P, 1])
        span_i = sb("span_i", [1, 1], I32)
        base_f = sb("base_f", [1, UNITS])
        base_m = sb("base_m", [1, UNITS])
        base_i = sb("base_i", [1, UNITS], I32)

        RB = 4 * UNIT
        rows_i = [z[1][:, i * RB:(i + 1) * RB].bitcast(I32).rearrange("p (b e) -> p b e", b=4)
                  for i in range(2)]
        rows_f = [z[1][:, (2 + i) * RB:(3 + i) * RB].rearrange("p (b e) -> p b e", b=4) for i in range(2)]

        ps_sum = [psum(f"ps_sum{i}", [P, 2, UPG, WIN]) for i in range(2)]
        ps_node = [psum(f"ps_node{i}", [P, CH * D]) for i in range(2)]
        ps_hT = [psum(f"ps_hT{i}", [P, 512]) for i in range(2)]
        ps_tr = psum("ps_tr", [P, 1024])

        consts_loaded = sem("consts_loaded")
        rows_loaded = sem("rows_loaded")
        rows_padded = sem("rows_padded")
        pool_consts = sem("pool_consts")
        z_cleared = sem("z_cleared")
        rows_float = sem("rows_float")
        tr_ready = sem("tr_ready")
        tr_read = sem("tr_read")
        diag_ready = sem("diag_ready")
        rows_done = sem("rows_done")
        dve_steps = sem("dve_steps")
        round_steps = sem("round_steps")
        x_loaded = sem("x_loaded")
        x1_ready = sem("x1_ready")
        x1_stored = sem("x1_stored")
        centered = sem("centered")
        squared = sem("squared")
        var_ready = sem("var_ready")
        std_ready = sem("std_ready")
        normed = sem("normed")
        h_ready = sem("h_ready")
        hT_turned = sem("hT_turned")
        hT_placed = sem("hT_placed")
        stored = [sem(f"stored{i}") for i in range(2)]
        out_ready = sem("out_ready")
        out_stored = sem("out_stored")
        out_free = sem("out_free")
        idx_ready = sem("idx_ready")
        msg_ready = [sem(f"msg_ready{i}") for i in range(RING)]
        attr_ready = [sem(f"attr_ready{i}") for i in range(RING)]
        onehot_ready = sem("onehot_ready")
        summed = sem("summed")
        sums_added = sem("sums_added")
        base_ready = sem("base_ready")
        scaled = sem("scaled")
        node_ready = sem("node_ready")
        node_read = sem("node_read")
        hT_ready = sem("hT_ready")
        hT_read = sem("hT_read")
        r_scaled = sem("r_scaled")

        W_SAGE = [("L0_gnn_w_self1", "L0_gnn_w_nei1"), ("L0_gnn_w_self2", "L0_gnn_w_nei2"),
                  ("L0_gnn_w_self3", "L0_gnn_w_nei3")]
        W_EDGE = ["L1_gnn_W1", "L1_gnn_W2"]
        BIAS = ["L0_gnn_b1", "L0_gnn_b2", "L0_gnn_b3", "L1_gnn_b1", "L1_gnn_b2"]
        N_CONSTS = 2 * 3 + 2 * 2 + 2 * LAYERS
        N_ROWS = 6
        HT_STAGE = {0: 0, 1: 1, 3: 2}
        N_HT = 2 * CHUNKS
        LN_STAGE = {-1: 0, 2: 1}
        X_STAGE = {-1: 0, 2: 1, 4: 2}
        STORE_STAGE = {-1: 0, 0: 1, 1: 2, 2: 3, 3: 4}

        def rows_of(t):
            return t.rearrange("(p j) f -> p j f", j=NODES_PP)

        def by_node(buf, lo, hi, j):
            return buf[lo:hi, 0:NPAD].rearrange("k (p j) -> k p j", j=NODES_PP)[:, :, j]

        def by_places(buf, lo, hi, j, n):
            return buf[lo:hi, 0:NPAD].rearrange("k (p j) -> k p j", j=NODES_PP)[:, :, bass.ds(j, n)]

        def rounds_of(eng):
            eng.wait_ge(base_ready, 1)
            span = eng.value_load(span_i[0:1, 0:1], min_val=0, max_val=N)
            return eng.snap(span // WIN + 1, min_val=1, max_val=N // WIN + 1)

        block = ctx.enter_context(nc.Block())

        @block.sync
        def _(sp):
            for lst, name in ((0, "src"), (1, "dst")):
                full = FULL_BLOCKS * P * UNIT
                sp.dma_start(rows_i[lst][:, 0:FULL_BLOCKS, :],
                             a[name][0:full].rearrange("(b p e) -> p b e", p=P, e=UNIT)).then_inc(rows_loaded, 16)
            sp.wait_ge(rows_padded, 1)
            for lst, name in ((0, "src"), (1, "dst")):
                full = FULL_BLOCKS * P * UNIT
                rest = full + TAIL_FULL * UNIT
                sp.dma_start(rows_i[lst][0:TAIL_FULL, 3, :],
                             a[name][full:rest].rearrange("(p e) -> p e", e=UNIT)).then_inc(rows_loaded, 16)
                sp.dma_start(rows_i[lst][TAIL_FULL:TAIL_FULL + 1, 3, 0:TAIL_REST],
                             a[name][rest:E].rearrange("(p e) -> p e", p=1)).then_inc(rows_loaded, 16)

            def load_rows(layer):
                padded = layer == 4
                t = x1_dram if padded else a["x"]
                for k in range(BODIES):
                    body = X_STAGE[layer] * BODIES + k
                    if body > 0:
                        sp.wait_ge(centered if body <= 2 * BODIES else out_ready, body if body <= 2 * BODIES else 2 * (body - 2 * BODIES))
                    if layer == 2 and k > 0:
                        sp.wait_ge(x1_stored, 16 * k)
                    src = t[0:LAST_P * NODES_PP, :].rearrange("(p j) f -> p j f", j=NODES_PP)
                    js = slice(k * BODY, (k + 1) * BODY)
                    sp.dma_start(xin[0:XSPLIT, :, :], src[0:XSPLIT, js, :]).then_inc(x_loaded, 16)
                    sp.dma_start(xin[XSPLIT:LAST_P, :, :], src[XSPLIT:LAST_P, js, :]).then_inc(x_loaded, 16)
                    lo = LAST_P * NODES_PP + k * BODY
                    n = min(BODY, N - lo)
                    if n <= 0:
                        lo, n = 0, BODY
                    sp.dma_start(xin[LAST_P:P, 0:n, :], t[lo:lo + n, :].rearrange("(o j) f -> o j f", o=1)
                                 ).then_inc(x_loaded, 16)
                    if layer == 2:
                        sp.wait_ge(x1_ready, k + 1)
                        sp.dma_start(rows_of(x1_dram)[:, js, :], xin[:, :, :]).then_inc(x1_stored, 16)
                    if layer == 2 or layer == -1:
                        for b in range(2):
                            store_chunk(layer, k, b)
                    if layer == 4:
                        for b in range(2):
                            store_out(k, b)

            def store_chunk(layer, k, b):
                sp.wait_ge(h_ready, STORE_STAGE[layer] * CHUNKS + 2 * k + b + 1)
                sp.dma_start(rows_of(table[(layer + 1) % 2])[:, bass.ds(BODY * k + CH * b, CH), :],
                             hbuf[:, b, :, :]).then_inc(stored[b], 16)

            outs = [0]

            def store_out(k, b):
                q = 2 * k + b
                sp.wait_ge(out_ready, q + 1)
                dst = out[0:LAST_P * NODES_PP, :].rearrange("(p j) f -> p j f", j=NODES_PP)
                js = slice(q * CH, (q + 1) * CH)
                sp.dma_start(dst[0:XSPLIT, js, :], hbuf[0:XSPLIT, b, :, :]).then_inc(out_stored, 16)
                sp.dma_start(dst[XSPLIT:LAST_P, js, :], hbuf[XSPLIT:LAST_P, b, :, :]).then_inc(out_stored, 16)
                outs[0] += 32
                n = min(CH, LAST_NODES - q * CH)
                if n > 0:
                    lo = LAST_P * NODES_PP + q * CH
                    sp.dma_start(out[lo:lo + n, :].rearrange("(o j) f -> o j f", o=1),
                                 hbuf[LAST_P:P, b, 0:n, :]).then_inc(out_stored, 16)
                    outs[0] += 16
                sp.wait_ge(out_stored, outs[0])
                sp.sem_inc(out_free, 1)

            load_rows(-1)
            for n, (ws, wn) in enumerate(W_SAGE):
                sp.dma_start(wcat[0:D, n, :], a[ws]).then_inc(consts_loaded, 16)
                sp.dma_start(wcat[D:P, n, :], a[wn]).then_inc(consts_loaded, 16)
            for n, w in enumerate(W_EDGE):
                sp.dma_start(wcat[:, 3 + n, :], a[w][0:P, :]).then_inc(consts_loaded, 16)
                sp.dma_start(wr[0:D, n, :], a[w][P:P + D, :]).then_inc(consts_loaded, 16)
            for n, w in enumerate(BIAS):
                sp.dma_start(bias_bc[:, n, :], a[w].rearrange("(o f) -> o f", o=1).to_broadcast([P, D])
                             ).then_inc(consts_loaded, 16)
                sp.dma_start(bias_col[:, n:n + 1], a[w].rearrange("(f o) -> f o", o=1)
                             ).then_inc(consts_loaded, 16)

            rounds = rounds_of(sp)

            def attr_group(it, g, i):
                sp.wait_ge(summed, 4 * it + g + 1)
                static = isinstance(i, int)
                for_last = static and (RING * i + g) * UPG >= FULL_BLOCKS * P + TAIL_FULL
                e0 = (RING * i + g) * (UPG * UNIT)
                dst = msg[:, g, :, 0:D]
                if for_last:
                    sp.dma_start(dst[0:TAIL_REST // TILES, 0:TILES, :],
                                 a["edge_attr_64"][E - TAIL_REST:E, :].rearrange("(p j) f -> p j f", j=TILES)
                                 ).then_inc(attr_ready[g], 32)
                    return
                rows = a["edge_attr_64"][bass.ds(e0, UPG * UNIT), :]
                for u in range(UPG):
                    sp.dma_start(dst[:, u * TILES:(u + 1) * TILES, :],
                                 rows[u * UNIT:(u + 1) * UNIT, :].rearrange("(p j) f -> p j f", j=TILES)
                                 ).then_inc(attr_ready[g], 16)

            with sp.Fori(0, rounds) as r:
                with sp.Fori(0, ITERS - 1) as i:
                    for g in range(RING):
                        attr_group(r * ITERS + i, g, i)
                for g in range(RING):
                    attr_group(r * ITERS + (ITERS - 1), g, ITERS - 1)

            for layer in range(LAYERS):
                if layer in (2, 4):
                    load_rows(layer)
                else:
                    with sp.Fori(0, BODIES) as k:
                        for b in range(2):
                            store_chunk(layer, k, b)
            sp.wait_ge(x1_stored, 16 * BODIES)
            for b in range(2):
                sp.wait_ge(stored[b], 16 * BODIES * len(STORE_STAGE))

        @block.gpsimd
        def _(pool):
            pool.memset(ident[:], 0.0).then_inc(pool_consts, 1)
            pool.memset(ones[:], 1.0).then_inc(pool_consts, 1)
            pool.wait_ge(pool_consts, 2)
            pool.affine_select(out=ident[:], in_=ident[:], compare_op=ALU.not_equal, fill=1.0, base=0,
                               pattern=[[-1, P]], channel_multiplier=1).then_inc(pool_consts, 1)
            pool.iota(iota[:], [[1, WIN]], base=0, channel_multiplier=0,
                      allow_small_or_imprecise_dtypes=True).then_inc(pool_consts, 1)
            pool.memset(zeros[:], 0.0).then_inc(pool_consts, 1)
            pool.memset(eps[:], EPS).then_inc(pool_consts, 1)
            pool.wait_ge(pool_consts, 6)
            pool.memset(wr[D:P, :, :], 0.0).then_inc(pool_consts, 1)
            pool.wait_ge(pool_consts, 7)
            pool.memset(z[0][D:P, :], 0.0).then_inc(z_cleared, 1)
            pool.wait_ge(z_cleared, 1)
            pool.memset(rd[:], 0.0).then_inc(z_cleared, 1)
            pool.wait_ge(z_cleared, 2)
            pool.wait_ge(rows_done, 1)
            pool.memset(z[1][0:D, :], 0.0).then_inc(z_cleared, 1)
            pool.wait_ge(z_cleared, 3)
            rounds = rounds_of(pool)
            for layer in range(LAYERS):
                for b in range(2):
                    pool.wait_ge(stored[b], 16 * BODIES * (layer + 1))
                pool.nop(nofuse=True)
                with pool.Fori(0, rounds) as r:
                    with pool.Fori(0, ITERS) as i:
                        it = (rounds * layer + r) * ITERS + i
                        for g in range(RING):
                            pool.wait_ge(idx_ready, 4 * it + g + 1)
                            pool.nop(nofuse=True)
                            for t in range(TPG):
                                pool.indirect_dma_start(
                                    out=msg[:, g, t, D:2 * D], out_offset=None,
                                    in_=table[layer % 2][:, :],
                                    in_offset=bass.IndirectOffsetOnAxis(ap=idx[:, g, t:t + 1], axis=0),
                                ).then_inc(msg_ready[g], 16)

        @block.tensor
        def _(pe):
            pe.sem_inc(summed, RING)
            pe.wait_ge(pool_consts, 7)
            turned = 0
            for lst in range(2):
                for blk in range(4):
                    n = P if blk < FULL_BLOCKS else TAIL_UNITS
                    if turned == 0:
                        pe.wait_ge(rows_float, 1)
                    if turned == 4:
                        pe.wait_ge(rows_float, 2)
                    if turned >= 2:
                        pe.wait_ge(tr_read, turned - 1)
                    for j in range(TILES):
                        last = nc.tensor.transpose(
                            ps_hT[turned % 2][:, j * P:j * P + n],
                            rows_f[lst][0:n, blk, :].rearrange("s (p j) -> s p j", j=TILES)[:, :, j],
                            ident[0:n, 0:n])
                    last.then_inc(tr_ready, 1)
                    turned += 1
            for blk in range(4):
                n = P if blk < FULL_BLOCKS else TAIL_UNITS
                pe.wait_ge(diag_ready, blk + 1)
                nc.tensor.matmul(ps_tr[:, blk * P:blk * P + n], ones[0:n, :], diag[0:n, 0:n],
                                 start=True, stop=True).then_inc(tr_ready, 1)
            nc.tensor.transpose(ps_tr[0:1, 512:512 + P], pspan[:, 0:1], ident[:]).then_inc(tr_ready, 1)

            placed = [0]

            def turn_body(layer, k):
                for b in range(2):
                    q = LN_STAGE[layer] * CHUNKS + 2 * k + b
                    pe.wait_ge(h_ready, STORE_STAGE[layer] * CHUNKS + 2 * k + b + 1)
                    pe.wait_ge(hT_placed, q + 1)
                    pe.nop(nofuse=True)
                    for j in range(CH):
                        last = nc.tensor.transpose(ps_tr[0:D, j * P:(j + 1) * P], hbuf[:, b, j, :], ident[:])
                    last.then_inc(hT_turned, 1)

            pe.wait_ge(base_ready, 1)
            turn_body(-1, 0)
            with pe.Fori(1, BODIES) as k:
                turn_body(-1, k)
            rounds = rounds_of(pe)
            pe.wait_ge(consts_loaded, 16 * N_CONSTS)
            for layer in range(LAYERS):
                cur = layer % 2
                lo = 0 if layer == 0 else D
                with pe.Fori(0, rounds) as r:
                    with pe.Fori(0, ITERS) as i:
                        it = (rounds * layer + r) * ITERS + i
                        for g in range(RING):
                            n = 4 * it + g
                            ps = ps_sum[g % 2]
                            pe.wait_ge(onehot_ready, n + 1)
                            pe.wait_ge(sums_added, 2 * n + 2)
                            pe.wait_ge(msg_ready[g], 16 * TPG * (it + 1))
                            if layer == 0:
                                pe.wait_ge(attr_ready[g], 32 * (it + 1))
                            for u in range(UPG):
                                for j in range(TILES if layer == 0 else 0):
                                    nc.tensor.matmul(ps[:, 1, u, :], ones[:, :], onehot[:, g % 2, u * TILES + j, :],
                                                     start=j == 0, stop=j == TILES - 1)
                                for j in range(TILES):
                                    t = u * TILES + j
                                    if layer == 0:
                                        to, what = ps[:, 0, u, :], msg[:, g, t, :]
                                    else:
                                        to, what = ps[D:P, 0, u, :], msg[:, g, t, D:2 * D]
                                    last = nc.tensor.matmul(to, what, onehot[:, g % 2, t, :],
                                                            start=j == 0, stop=j == TILES - 1)
                            last.then_inc(summed, 1)
                if layer in (1, 2, 4):
                    pe.wait_ge(hT_read, 2 + N_HT * (HT_STAGE[layer - 1] + 1))
                else:
                    pe.wait_ge(hT_placed, 1 + CHUNKS * (LN_STAGE[-1 if layer == 0 else 2] + 1))
                for k in range(BODIES):
                    for b in range(2):
                        m = CHUNKS * layer + 2 * k + b
                        pe.wait_ge(scaled, m + 1)
                        pe.wait_ge(node_read, m + 1)
                        for j in range(CH):
                            o = ps_node[b][:, j * D:(j + 1) * D]
                            at = BODY * k + (CH * b + j)
                            last = nc.tensor.matmul(o, by_node(z[cur], 0, P, at), wcat[:, layer, :],
                                                    start=True, stop=layer < 3)
                            if layer >= 3:
                                last = nc.tensor.matmul(o, by_node(rd, 0, D, at), wr[0:D, layer - 3, :],
                                                        start=False, stop=True)
                        last.then_inc(node_ready, 1)
                    if layer == 2:
                        turn_body(layer, k)
                if layer in HT_STAGE:
                    with pe.Fori(0, N_HT // 2) as k:
                        for b in range(2):
                            m = N_HT * HT_STAGE[layer] + 2 * k + b
                            cols = bass.ds(2 * TCOLS * k + TCOLS * b, TCOLS)
                            pe.wait_ge(hT_read, m + 1)
                            last = nc.tensor.matmul(ps_hT[b][0:D, 0:TCOLS], wcat[:, layer, :], z[cur][:, cols],
                                                    start=True, stop=layer < 3)
                            if layer >= 3:
                                last = nc.tensor.matmul(ps_hT[b][0:D, 0:TCOLS], wr[:, layer - 3, :], rd[:, cols],
                                                        start=False, stop=True)
                            last.then_inc(hT_ready, 1)

        @block.vector
        def _(dve):
            dve.sem_inc(out_free, 2)
            steps = Steps(dve, dve_steps)
            dve.sem_inc(sums_added, SUMS_CREDIT)
            dve.sem_inc(node_read, 2)
            nc.vector.memset(rows_i[0][0:TAIL_UNITS, 3, :], 0)
            nc.vector.memset(rows_i[1][0:TAIL_UNITS, 3, :], N).then_inc(rows_padded, 1)
            nc.vector.memset(dlow[:], 0.0)
            steps.done(nc.vector.memset(dhigh[:], 0.0))
            dve.wait_ge(rows_loaded, 16 * N_ROWS)
            for lst in range(2):
                nc.vector.tensor_copy(rows_f[lst][:, 0:FULL_BLOCKS, :], rows_i[lst][:, 0:FULL_BLOCKS, :])
                nc.vector.tensor_copy(rows_f[lst][0:TAIL_UNITS, 3, :], rows_i[lst][0:TAIL_UNITS, 3, :]
                                      ).then_inc(rows_float, 1)
            for lst, to in ((0, src_t), (1, dst_t)):
                for blk in range(4):
                    n = P if blk < FULL_BLOCKS else TAIL_UNITS
                    dve.wait_ge(tr_ready, 4 * lst + blk + 1)
                    cols = to[:, blk * UNIT:blk * UNIT + n * TILES].rearrange("p (s j) -> p j s", j=TILES)
                    last = nc.vector.tensor_copy(
                        cols, ps_hT[(4 * lst + blk) % 2][:].rearrange("p (j s) -> p j s", j=TILES)[:, :, 0:n])
                    last.then_inc(tr_read, 1)
            dve.wait_ge(rows_float, 2)
            for at, op in ((dlow, ALU.min), (dhigh, ALU.max)):
                nc.vector.tensor_reduce(at[:, 0:FULL_BLOCKS], rows_f[1][:, 0:FULL_BLOCKS, :], AX_X, op)
                last = nc.vector.tensor_reduce(at[0:TAIL_UNITS, 3:4], rows_f[1][0:TAIL_UNITS, 3, :], AX_X, op)
            last.then_inc(rows_done, 1)
            dve.wait_ge(rows_done, 1)
            steps.done(nc.vector.tensor_tensor(dspan[:], dhigh[:], dlow[:], ALU.subtract))
            steps.done(nc.vector.tensor_reduce(pspan[:, 0:1], dspan[:], AX_X, ALU.max))
            for blk in range(4):
                n = P if blk < FULL_BLOCKS else TAIL_UNITS
                if blk:
                    dve.wait_ge(tr_ready, 8 + blk)
                else:
                    dve.wait_ge(pool_consts, 7)
                nc.vector.tensor_scalar(diag[0:n, 0:n], ident[0:n, 0:n], dlow[0:n, blk:blk + 1], None,
                                        ALU.mult).then_inc(diag_ready, 1)
            dve.wait_ge(tr_ready, 13)
            by_unit = dst_t[:].rearrange("p (s j) -> p s j", j=TILES)
            nc.vector.tensor_tensor(by_unit, by_unit, ps_tr[:, 0:UNITS].unsqueeze(2).to_broadcast([P, UNITS, TILES]),
                                    ALU.subtract)
            steps.done(nc.vector.tensor_copy(base_f[:], ps_tr[0:1, 0:UNITS]))
            steps.done(nc.vector.tensor_reduce(shift[0:1, 0:1], ps_tr[0:1, 512:512 + P], AX_X, ALU.max))
            nc.vector.tensor_copy(span_i[:], shift[0:1, 0:1]).then_inc(base_ready, 1)

            def layernorm(layer, k):
                body = LN_STAGE[layer] * BODIES + k
                if layer == -1:
                    dve.wait_ge(x_loaded, 48 * (k + 1))
                steps.done(nc.vector.tensor_reduce(mean[:], xin[:], AX_X, ALU.add))
                steps.done(nc.vector.tensor_scalar(mean[:], mean[:], 1.0 / D, None, ALU.mult))
                if not (isinstance(body, int) and body == 0):
                    dve.wait_ge(h_ready, STORE_STAGE[layer] * CHUNKS + 2 * k)
                nc.vector.tensor_tensor(cent[:], xin[:], mean[:].unsqueeze(2).to_broadcast([P, BODY, D]),
                                        ALU.subtract).then_inc(centered, 1)
                dve.wait_ge(squared, body + 1)
                nc.vector.tensor_reduce(var[:], vbuf[:], AX_X, ALU.add).then_inc(var_ready, 1)
                dve.wait_ge(std_ready, body + 1)
                steps.done(nc.vector.reciprocal(mean[:], std[:]))
                nc.vector.tensor_tensor(cent[:], cent[:], mean[:].unsqueeze(2).to_broadcast([P, BODY, D]),
                                        ALU.mult).then_inc(normed, 1)

            layernorm(-1, 0)
            steps.leave(0)
            with dve.Fori(1, BODIES) as k:
                steps.enter(3, k - 1)
                layernorm(-1, k)
            steps.leave(BODIES - 1)

            rounds = rounds_of(dve)
            dve.wait_ge(z_cleared, 3)
            dve.wait_ge(consts_loaded, 16 * N_CONSTS)
            for layer in range(LAYERS):
                cur, nxt = layer % 2, (layer + 1) % 2
                steps.done(nc.vector.memset(shift[:], 0.0))
                with dve.Fori(0, rounds) as r:
                    rnd = rounds * layer + r
                    nc.vector.tensor_scalar(iota_r[:], iota[:], shift[:, 0:1], None, ALU.add)
                    nc.vector.tensor_scalar(base_m[:], base_f[:], shift[0:1, 0:1], float(N),
                                            ALU.add, ALU.min).then_inc(round_steps, 1)
                    dve.wait_ge(round_steps, 2 * rnd + 1)
                    nc.vector.tensor_scalar(shift[:], shift[:], float(WIN), None, ALU.add)
                    nc.vector.tensor_copy(base_i[:], base_m[:]).then_inc(round_steps, 1)
                    dve.wait_ge(round_steps, 2 * rnd + 2)
                    dve.nop(nofuse=True)
                    with dve.Fori(0, ITERS) as i:
                        _, bases = nc.values_load_multi_w_load_instructions(
                            base_i[0:1, bass.ds(RING * UPG * i, RING * UPG)], engines=[mybir.EngineType.DVE],
                            min_val=0, max_val=N, skip_runtime_bounds_check_because="held at N above")
                        for g in range(RING):
                            n = 4 * (rnd * ITERS + i) + g
                            dsts = dst_t[:, bass.ds(RING * TPG * i + TPG * g, TPG)]
                            nc.vector.tensor_tensor(
                                onehot[:, g % 2, :, :], dsts.unsqueeze(2).to_broadcast([P, TPG, WIN]),
                                iota_r[:].unsqueeze(1).to_broadcast([P, TPG, WIN]), ALU.is_equal
                            ).then_inc(onehot_ready, 1)
                            dve.wait_ge(summed, RING + n + 1)
                            for u in range(UPG):
                                dve.wait_ge(sums_added, SUMS_CREDIT + 2 * n + u)
                                cols = bass.ds(bases[g * UPG + u], WIN)
                                to = [(z[cur], D, P, 0)]
                                if layer == 0:
                                    to += [(rd, D, P, 1), (rd, 0, D, 0), (z[1], 0, D, 1)]
                                for buf, lo, hi, kind in to:
                                    last = nc.vector.tensor_tensor(buf[lo:hi, cols], buf[lo:hi, cols],
                                                                   ps_sum[g % 2][lo:hi, kind, u, :], ALU.add)
                                last.then_inc(sums_added, 1)
                dve.wait_ge(sums_added, rounds * (2 * GROUPS * (layer + 1)) + SUMS_CREDIT)
                dve.nop(nofuse=True)
                if layer == 0:
                    steps.done(nc.vector.tensor_scalar(rd[D:P, :], rd[D:P, :], 1.0, None, ALU.max))
                    steps.done(nc.vector.reciprocal(rd[D:P, :], rd[D:P, :]))
                if layer == 4:
                    for b in range(2):
                        dve.wait_ge(stored[b], 16 * BODIES * len(STORE_STAGE))
                with dve.Fori(0, BODIES) as k:
                    if layer == 2:
                        steps.enter(3, k)
                    for b in range(2):
                        at = BODY * k + CH * b
                        means = by_places(z[cur], D, P, at, CH)
                        nc.vector.tensor_tensor(means, means, by_places(rd, D, P, at, CH), ALU.mult
                                                ).then_inc(scaled, 1)
                    for b in range(2):
                        m = CHUNKS * layer + 2 * k + b
                        v = vbuf[:, b * CH:(b + 1) * CH, :]
                        dve.wait_ge(node_ready, m + 1)
                        if layer < 4:
                            dve.wait_ge(h_ready, CHUNKS * (layer + 1) + 2 * k + (b - 1 if layer != 2 else 0))
                        ins = nc.vector.tensor_tensor(
                            v, ps_node[b][:].rearrange("p (c f) -> p c f", f=D),
                            bias_bc[:, layer, :].unsqueeze(1).to_broadcast([P, CH, D]), ALU.add)
                        ins.then_inc(node_read, 1)
                        if layer == 4:
                            dve.wait_ge(node_read, 2 + m + 1)
                            dve.wait_ge(out_free, 2 * k + b + 1)
                            if b == 0:
                                dve.wait_ge(x_loaded, 48 * (2 * BODIES + k + 1))
                            nc.vector.scalar_tensor_tensor(
                                out=hbuf[:, b, :, :], in0=v, scalar=0.0, in1=xin[:, b * CH:(b + 1) * CH, :],
                                op0=ALU.max, op1=ALU.add).then_inc(out_ready, 1)
                    if layer == 2:
                        dve.wait_ge(node_read, 2 + CHUNKS * layer + 2 * k + 2)
                        dve.wait_ge(x_loaded, 48 * (BODIES + k + 1))
                        ins = nc.vector.tensor_tensor(xin[:], xin[:], vbuf[:], ALU.add)
                        ins.then_inc(x1_ready, 1)
                        dve.wait_ge(x1_ready, k + 1)
                        layernorm(2, k)
                if layer == 2:
                    steps.leave(BODIES)
                if layer == 0:
                    steps.done(nc.vector.tensor_scalar(z[1][0:D, :], z[1][0:D, :], 1.0, None, ALU.max))
                    steps.done(nc.vector.reciprocal(z[1][0:D, :], z[1][0:D, :]))
                    nc.vector.tensor_tensor(rd[0:D, :], rd[0:D, :], z[1][0:D, :], ALU.mult).then_inc(r_scaled, 1)

        @block.scalar
        def _(act):
            act.sem_inc(hT_read, 2)
            act.sem_inc(hT_placed, 1)
            act.wait_ge(pool_consts, 7)

            def layernorm(layer, k):
                body = LN_STAGE[layer] * BODIES + k
                act.wait_ge(centered, body + 1)
                nc.scalar.activation(vbuf[:], cent[:], ACT.Square).then_inc(squared, 1)
                act.wait_ge(var_ready, body + 1)
                nc.scalar.activation(std[:], var[:], ACT.Sqrt, bias=eps[:, 0:1], scale=1.0 / D
                                     ).then_inc(std_ready, 1)
                act.wait_ge(normed, body + 1)
                for b in range(2):
                    relu_chunk(layer, k, b, cent)
                for b in range(2):
                    q = LN_STAGE[layer] * CHUNKS + 2 * k + b
                    act.wait_ge(hT_turned, q + 1)
                    nc.scalar.copy(
                        by_places(z[(layer + 1) % 2], 0, D, BODY * k + CH * b, CH).rearrange("f p j -> f j p"),
                        ps_tr[0:D, 0:CH * P].rearrange("f (j p) -> f j p", j=CH)).then_inc(hT_placed, 1)

            def relu_chunk(layer, k, b, src):
                before = STORE_STAGE[layer] * BODIES + k
                if not (isinstance(before, int) and before == 0):
                    act.wait_ge(stored[b], 16 * before)
                nc.scalar.activation(hbuf[:, b, :, :], src[:, b * CH:(b + 1) * CH, :], ACT.Relu
                                     ).then_inc(h_ready, 1)

            layernorm(-1, 0)
            with act.Fori(1, BODIES) as k:
                layernorm(-1, k)

            rounds = rounds_of(act)
            for layer in range(LAYERS):
                cur, nxt = layer % 2, (layer + 1) % 2
                with act.Fori(0, rounds) as r:
                    with act.Fori(0, ITERS) as i:
                        it = (rounds * layer + r) * ITERS + i
                        for g in range(RING):
                            act.wait_ge(summed, 4 * it + g + 1)
                            nc.scalar.copy(idx[:, g, :], src_t[:, bass.ds(RING * TPG * i + TPG * g, TPG)]
                                           ).then_inc(idx_ready, 1)
                        if layer < 4:
                            nc.scalar.copy(z[nxt][D:P, bass.ds(ZPIECE * i, ZPIECE)], zeros[D:P, :])
                if layer < 4:
                    with act.Fori(0, BODIES) as k:
                        if layer == 2:
                            layernorm(layer, k)
                        else:
                            for b in range(2):
                                act.wait_ge(node_read, 2 + CHUNKS * layer + 2 * k + b + 1)
                                relu_chunk(layer, k, b, vbuf)
                if layer in HT_STAGE:
                    if layer == 0:
                        act.wait_ge(r_scaled, 1)
                    with act.Fori(0, N_HT // 2) as k:
                        for b in range(2):
                            m = N_HT * HT_STAGE[layer] + 2 * k + b
                            act.wait_ge(hT_ready, m + 1)
                            nc.scalar.activation(z[nxt][0:D, bass.ds(2 * TCOLS * k + TCOLS * b, TCOLS)],
                                                 ps_hT[b][0:D, 0:TCOLS], ACT.Relu,
                                                 bias=bias_col[:, layer:layer + 1]).then_inc(hT_read, 1)


_INS = ["x", "src", "dst", "edge_attr_64", "L0_gnn_w_self1", "L0_gnn_w_nei1", "L0_gnn_b1", "L0_gnn_w_self2",
        "L0_gnn_w_nei2", "L0_gnn_b2", "L0_gnn_w_self3", "L0_gnn_w_nei3", "L0_gnn_b3", "L1_gnn_W1", "L1_gnn_b1",
        "L1_gnn_W2", "L1_gnn_b2"]


def kernel(**inputs):
    import numpy as np
    import concourse.bacc as bacc
    from concourse.bass_utils import run_bass_kernel_spmd

    nc = bacc.Bacc("TRN2", target_bir_lowering=False, num_devices=1)
    arrays, aps = {}, {}
    for name in _INS:
        v = np.ascontiguousarray(inputs[name])
        arrays[f"in_{name}"] = v
        aps[name] = nc.dram_tensor(f"in_{name}", v.shape, mybir.dt.from_np(v.dtype), kind="ExternalInput").ap()
    out = nc.dram_tensor("out_0", (N, D), F32, kind="ExternalOutput").ap()
    program(nc, aps, out)
    r = run_bass_kernel_spmd(nc, [arrays], core_ids=[0])
    return r.results[0]["out_0"]
```

```python
from contextlib import ExitStack

import concourse.bass as bass
from concourse import mybir

F32 = mybir.dt.float32
I32 = mybir.dt.int32
U32 = mybir.dt.uint32
ALU = mybir.AluOpType
ACT = mybir.ActivationFunctionType
AX_X = mybir.AxisListType.X
DVE_ONLY = [mybir.EngineType.DVE]

P = 128
N = 12500
E = 200000
D = 64
EPS = 1e-05
TILES = 4
UNIT = P * TILES
WIN = 64
UPG = 2
TPG = UPG * TILES
RING = 4
ITERS = -(-E // (UNIT * UPG * RING))
GROUPS = ITERS * RING
UNITS = GROUPS * UPG
NODE_TILES = 2 * -(-N // (2 * P))
NPAD = P * NODE_TILES
STEP_TILES = 2
STEP_NODES = P * STEP_TILES
STEPS = NODE_TILES // STEP_TILES
EARLY = STEPS - 1
EARLY_AT = 3
NODES_PER_UNIT = NPAD // UNITS
ZPIECE = -(-(N + WIN) // ITERS)
ZW = ITERS * ZPIECE
assert ITERS == STEPS and ZW >= NPAD and NPAD == UNITS * NODES_PER_UNIT
LAST_ROWS = N - P * (NODE_TILES - 1)
PIECES = 7
PT = NODE_TILES // PIECES
PC = PT * D
LAYERS = 5
FULL_BLOCKS = E // (P * UNIT)
BLOCKS = FULL_BLOCKS + 1
TAIL_UNITS = UNITS - FULL_BLOCKS * P
TAIL_FULL = (E - FULL_BLOCKS * P * UNIT) // UNIT
TURNS = -(-NODE_TILES // 4)
TAIL_REST = E - (FULL_BLOCKS * P + TAIL_FULL) * UNIT
ADD_CREDIT = 4
FAR = 32768.0


class Serial:

    def __init__(self, eng, sem, per, turn):
        self.eng, self.sem, self.per, self.turn, self.n = eng, sem, per, turn, 0

    def done(self, ins):
        self.n += 1
        ins.then_inc(self.sem, 1)
        self.eng.wait_ge(self.sem, self.turn * self.per + self.n)

    def end(self):
        assert self.n == self.per


def program(nc, a, out):
    with ExitStack() as ctx:
        def sb(name, shape, dt=F32):
            return ctx.enter_context(nc.sbuf_tensor(name, shape, dt))

        def psum(name, shape):
            return ctx.enter_context(nc.psum_tensor(name, shape, F32))

        def sem(name):
            return ctx.enter_context(nc.semaphore(name))

        table = [nc.dram_tensor(f"table{i}", (NPAD, D), F32).ap() for i in range(2)]
        x_dram = nc.dram_tensor("x_rows", (NPAD, D), F32).ap()
        x1_dram = nc.dram_tensor("x1_rows", (NPAD, D), F32).ap()

        z = [sb(f"z{i}", [P, ZW]) for i in range(2)]
        rd = sb("rd", [P, ZW])
        src_t = sb("src_t", [P, UNITS * TILES])
        dst_t = sb("dst_t", [P, UNITS * TILES + TPG])
        msg = sb("msg", [P, RING, TPG, 2 * D])
        idx = sb("idx", [P, RING, TPG], U32)
        onehot = sb("onehot", [P, 2, TPG, WIN])
        zs = sb("zs", [P, STEP_NODES])
        inv = sb("inv", [P, STEP_NODES])
        zr = sb("zr", [D, STEP_NODES])
        vbuf = sb("vbuf", [P, STEP_TILES, D])
        hbuf = sb("hbuf", [P, STEP_TILES, D])
        xs = sb("xs", [P, STEP_TILES, D])
        cent = sb("cent", [P, STEP_TILES, D])
        sq = sb("sq", [P, STEP_TILES, D])
        mean = sb("mean", [P, STEP_TILES])
        var = sb("var", [P, STEP_TILES])
        std = sb("std", [P, STEP_TILES])
        rstd = sb("rstd", [P, STEP_TILES])
        pre_mean = sb("pre_mean", [P, NODE_TILES])
        pre_var = sb("pre_var", [P, NODE_TILES])
        pre_std = sb("pre_std", [P, NODE_TILES])
        eps = sb("eps", [P, 1])
        ident = sb("ident", [P, P])
        ones = sb("ones", [P, P])
        diag = sb("diag", [P, P])
        iota = sb("iota", [P, WIN])
        iota_r = sb("iota_r", [P, WIN])
        shift = sb("shift", [P, 1])
        zeros = sb("zeros", [P, ZPIECE])
        wcat = sb("wcat", [P, LAYERS, D])
        wr = sb("wr", [D, 2, D])
        bias_bc = sb("bias_bc", [P, LAYERS, D])
        bias_col = sb("bias_col", [D, LAYERS])
        dlow = sb("dlow", [P, BLOCKS])
        dhigh = sb("dhigh", [P, BLOCKS])
        dspan = sb("dspan", [P, BLOCKS])
        dlate = sb("dlate", [P, BLOCKS])
        worst = sb("worst", [P, 2])
        worst_row = sb("worst_row", [1, 2])
        plan_f = sb("plan_f", [1, 3])
        plan_i = sb("plan_i", [1, 3], I32)
        base_f = sb("base_f", [1, UNITS])
        base_m = sb("base_m", [1, UNITS])
        base_i = sb("base_i", [1, UNITS], I32)

        LIST = BLOCKS * UNIT
        rows_f = [z[1][:, i * LIST:(i + 1) * LIST].rearrange("p (b e) -> p b e", b=BLOCKS) for i in range(2)]
        rows_i = [z[1][:, i * LIST:(i + 1) * LIST].bitcast(I32).rearrange("p (b e) -> p b e", b=BLOCKS)
                  for i in range(2)]
        XC = NODE_TILES * D
        assert 2 * XC <= ZW and 2 * LIST + XC <= ZW

        def by_tile(buf, lo):
            return buf[:, lo:lo + XC].rearrange("p (t f) -> p t f", f=D)

        pre_x, pre_c, pre_sq = by_tile(rd, 0), by_tile(rd, XC), by_tile(z[1], 2 * LIST)

        ps_sum = [psum(f"ps_sum{i}", [P, 2, UPG, WIN]) for i in range(2)]
        ps_node = psum("ps_node", [P, STEP_TILES, D])
        ps_hT = psum("ps_hT", [P, 512])
        ps_inv = psum("ps_inv", [P, 512])
        ps_tr = [psum(f"ps_tr{i}", [P, 512]) for i in range(2)]

        consts_loaded = sem("consts_loaded")
        rows_loaded = sem("rows_loaded")
        dve_padded = sem("dve_padded")
        pool_consts = sem("pool_consts")
        z_cleared = sem("z_cleared")
        limits_ready = sem("limits_ready")
        out_stored = sem("out_stored")
        rows_float = sem("rows_float")
        tr_ready = sem("tr_ready")
        tr_read = sem("tr_read")
        diag_ready = sem("diag_ready")
        plan_psum = sem("plan_psum")
        plan_ready = sem("plan_ready")
        dve_serial = sem("dve_serial")
        pre_loaded = [sem(f"pre_loaded{i}") for i in range(PIECES)]
        pre_centered = sem("pre_centered")
        pre_squared = sem("pre_squared")
        pre_summed = sem("pre_summed")
        pre_rooted = sem("pre_rooted")
        pre_normed = sem("pre_normed")
        pre_h = sem("pre_h")
        pre_stored = sem("pre_stored")
        turned = sem("turned")
        placed = sem("placed")
        x_copied = sem("x_copied")
        idx_ready = sem("idx_ready")
        msg_ready = [sem(f"msg_ready{i}") for i in range(RING)]
        attr_ready = [sem(f"attr_ready{i}") for i in range(RING)]
        msgs_reset = sem("msgs_reset")
        onehot_ready = sem("onehot_ready")
        summed = sem("summed")
        sums_added = sem("sums_added")
        windows_set = sem("windows_set")
        step_serial = [sem(f"step_serial{i}") for i in range(LAYERS)]
        inv_ready = sem("inv_ready")
        scaled = sem("scaled")
        h_copied = sem("h_copied")
        inv_low_ready = sem("inv_low_ready")
        r_ready = sem("r_ready")
        hT_ready = sem("hT_ready")
        hT_read = sem("hT_read")
        node_ready = sem("node_ready")
        node_read = sem("node_read")
        h_ready = sem("h_ready")
        hbuf_free = sem("hbuf_free")
        stored = sem("stored")
        x_loaded = {2: sem("x_loaded2"), 4: sem("x_loaded4")}
        x1_ready = sem("x1_ready")
        x1_stored = sem("x1_stored")
        centered = sem("centered")
        squared = sem("squared")
        var_ready = sem("var_ready")
        std_ready = sem("std_ready")
        normed = sem("normed")

        W_SAGE = [("L0_gnn_w_self1", "L0_gnn_w_nei1"), ("L0_gnn_w_self2", "L0_gnn_w_nei2"),
                  ("L0_gnn_w_self3", "L0_gnn_w_nei3")]
        W_EDGE = ["L1_gnn_W1", "L1_gnn_W2"]
        BIAS = ["L0_gnn_b1", "L0_gnn_b2", "L0_gnn_b3", "L1_gnn_b1", "L1_gnn_b2"]
        N_CONSTS = 2 * 3 + 2 * 2 + 2 * LAYERS
        POOL_CONSTS = 6
        SERIAL = {0: 1, 1: 1, 2: 4, 3: 1, 4: 1}

        class Plan:

            def __init__(self, eng):
                eng.wait_ge(plan_ready, 1)
                span = eng.value_load(plan_i[0:1, 0:1], min_val=0, max_val=N)
                self.rounds = eng.snap(span // WIN + 1, min_val=1, max_val=N // WIN + 1)
                self.left = eng.value_load(plan_i[0:1, 1:2], min_val=1, max_val=STEPS)
                self.left_last = eng.value_load(plan_i[0:1, 2:3], min_val=2, max_val=STEPS)
                self.steps = eng.snap(self.rounds * EARLY + self.left, min_val=1)

        def loops(eng, plan, layer, iteration, step, behind=0, peel_last=False):
            def early(r, tt):
                return lambda added: step(layer, tt, r * EARLY + tt, added)

            with eng.Fori(0, plan.rounds) as r:
                rnd = plan.rounds * layer + r
                for i in range(1 + behind):
                    iteration(layer, rnd, i, lambda added: None)
                with eng.Fori(0, EARLY - behind - peel_last) as tt:
                    iteration(layer, rnd, tt + 1 + behind, early(r, tt))
                if peel_last:
                    iteration(layer, rnd, ITERS - 1, early(r, EARLY - 1 - behind))
                if behind:
                    early(r, EARLY - 1)(None)
            added = plan.rounds * ((layer + 1) * GROUPS)
            here = plan.rounds * EARLY
            if layer < LAYERS - 1:
                with eng.Fori(0, plan.left) as k:
                    step(layer, EARLY - k, here + k, added)
            else:
                step(layer, EARLY, here, added)
                with eng.Fori(1, plan.left_last) as k:
                    step(layer, EARLY - k, here + k, added)

        def tiles_in(i, g):
            if not isinstance(i, int):
                return TPG
            units = [(i * RING + g) * UPG + u for u in range(UPG)]
            return TILES * sum(unit * UNIT < E for unit in units)

        def messages(g):
            return 16 * sum(tiles_in(i, g) for i in range(ITERS))

        def tile_rows(t, tt):
            return t[bass.ds(tt * STEP_NODES, STEP_NODES), :].rearrange("(t p) f -> p t f", p=P)

        block = ctx.enter_context(nc.Block())

        @block.sync
        def _(sp):
            full = FULL_BLOCKS * P * UNIT
            rest = full + TAIL_FULL * UNIT
            lists = (("dst", 1), ("src", 0))
            for name, at in lists:
                sp.dma_start(rows_i[at][:, 0:FULL_BLOCKS, :],
                             a[name][0:full].rearrange("(b p e) -> p b e", p=P, e=UNIT)).then_inc(rows_loaded, 16)
            sp.wait_ge(dve_padded, 1)
            for name, at in lists:
                sp.dma_start(rows_i[at][0:TAIL_FULL, FULL_BLOCKS, :],
                             a[name][full:rest].rearrange("(p e) -> p e", e=UNIT)).then_inc(rows_loaded, 16)
                sp.dma_start(rows_i[at][TAIL_FULL:TAIL_FULL + 1, FULL_BLOCKS, 0:TAIL_REST],
                             a[name][rest:E].rearrange("(p e) -> p e", p=1)).then_inc(rows_loaded, 16)
            for n, (ws, wn) in enumerate(W_SAGE):
                sp.dma_start(wcat[0:D, n, :], a[ws]).then_inc(consts_loaded, 16)
                sp.dma_start(wcat[D:P, n, :], a[wn]).then_inc(consts_loaded, 16)
            for n, w in enumerate(W_EDGE):
                sp.dma_start(wcat[:, 3 + n, :], a[w][0:P, :]).then_inc(consts_loaded, 16)
                sp.dma_start(wr[:, n, :], a[w][P:P + D, :]).then_inc(consts_loaded, 16)
            for n, w in enumerate(BIAS):
                sp.dma_start(bias_bc[:, n, :], a[w].rearrange("(o f) -> o f", o=1).to_broadcast([P, D])
                              ).then_inc(consts_loaded, 16)
                sp.dma_start(bias_col[:, n:n + 1], a[w].rearrange("(f o) -> f o", o=1)).then_inc(consts_loaded, 16)
            for k in range(PIECES):
                sp.wait_ge(pre_h, k + 1)
                sp.dma_start(table[0][k * PT * P:(k + 1) * PT * P, :].rearrange("(t p) f -> p t f", p=P),
                             pre_c[:, k * PT:(k + 1) * PT, :]).then_inc(pre_stored, 16)
            sp.dma_start(x_dram[0:N, :], a["x"][:, :]).then_inc(x_copied, 16)
            sp.wait_ge(pool_consts, POOL_CONSTS)
            sp.dma_start(x_dram[N:NPAD, :], zeros[0:NPAD - N, 0:D]).then_inc(x_copied, 16)
            sp.wait_ge(x_copied, 32)
            plan = Plan(sp)

            def iteration(layer, rnd, i, early):
                it = rnd * ITERS + i
                for g in range(RING):
                    if g == EARLY_AT:
                        early(None)
                    if layer:
                        continue
                    sp.wait_ge(summed, it * RING + g + 1)
                    for u in range(UPG):
                        unit = (i * RING + g) * UPG + u
                        n = P
                        if isinstance(i, int) and (unit + 1) * UNIT > E:
                            n = max(E - unit * UNIT, 0) // TILES
                            if n == 0:
                                n, unit = P, 0
                        sp.dma_start(msg[0:n, g, u * TILES:(u + 1) * TILES, 0:D],
                                     a["edge_attr_64"][bass.ds(unit * UNIT, n * TILES), :]
                                     .rearrange("(p j) f -> p j f", j=TILES)).then_inc(attr_ready[g], 16)

            def step(layer, tt, here, added):
                cnt = plan.steps * layer + here
                if layer in x_loaded:
                    sp.dma_start(xs[:], tile_rows(x_dram if layer == 2 else x1_dram, tt)).then_inc(x_loaded[layer], 16)
                if layer == 2:
                    sp.wait_ge(x1_ready, here + 1)
                    sp.dma_start(tile_rows(x1_dram, tt), xs[:]).then_inc(x1_stored, 16)
                sp.wait_ge(h_ready, cnt + 2)
                sp.nop(nofuse=True)
                if layer < LAYERS - 1:
                    sp.dma_start(tile_rows(table[(layer + 1) % 2], tt), hbuf[:]).then_inc(stored, 16)
                    sp.wait_ge(stored, 16 * (cnt + 1))
                elif isinstance(tt, int) and tt == EARLY:
                    lo = tt * STEP_NODES
                    sp.dma_start(out[lo:lo + P, :], hbuf[:, 0, :]).then_inc(out_stored, 16)
                    sp.dma_start(out[lo + P:N, :], hbuf[0:LAST_ROWS, 1, :]).then_inc(out_stored, 16)
                    sp.wait_ge(out_stored, 16 * (here + 2))
                else:
                    sp.dma_start(tile_rows(out, tt), hbuf[:]).then_inc(out_stored, 16)
                    sp.wait_ge(out_stored, 16 * (here + (1 if added is None else 2)))
                sp.sem_inc(hbuf_free, 1)
                if layer == 2:
                    sp.wait_ge(x1_stored, 16 * (here + 1))
                    sp.nop(nofuse=True)

            for layer in range(LAYERS):
                loops(sp, plan, layer, iteration, step, behind=1, peel_last=layer == 0)

        @block.gpsimd
        def _(pool):
            pool.memset(ident[:], 0.0).then_inc(pool_consts, 1)
            pool.memset(ones[:], 1.0).then_inc(pool_consts, 1)
            pool.wait_ge(pool_consts, 2)
            pool.affine_select(out=ident[:], in_=ident[:], compare_op=ALU.not_equal, fill=1.0, base=0,
                               pattern=[[-1, P]], channel_multiplier=1).then_inc(pool_consts, 1)
            pool.iota(iota[:], [[1, WIN]], base=0, channel_multiplier=0,
                      allow_small_or_imprecise_dtypes=True).then_inc(pool_consts, 1)
            pool.memset(zeros[:], 0.0).then_inc(pool_consts, 1)
            pool.memset(eps[:], EPS).then_inc(pool_consts, 1)
            pool.iota(dlate[:], [[NODES_PER_UNIT * P, BLOCKS]], base=-NODES_PER_UNIT * UPG * EARLY_AT,
                      channel_multiplier=NODES_PER_UNIT, allow_small_or_imprecise_dtypes=True).then_inc(limits_ready, 1)
            pool.wait_ge(pool_consts, POOL_CONSTS)
            pool.wait_ge(limits_ready, 1)
            pool.memset(z[0][D:P, :], 0.0).then_inc(z_cleared, 1)
            plan = Plan(pool)
            pool.wait_ge(pre_stored, 16 * PIECES)
            pool.nop(nofuse=True)

            def iteration(layer, rnd, i):
                for g in range(RING):
                    pool.wait_ge(idx_ready, (rnd * ITERS + i) * RING + g + 1)
                    pool.nop(nofuse=True)
                    for t in range(tiles_in(i, g)):
                        pool.indirect_dma_start(
                            out=msg[:, g, t, D:2 * D], out_offset=None, in_=table[layer % 2][:, :],
                            in_offset=bass.IndirectOffsetOnAxis(ap=idx[:, g, t:t + 1], axis=0),
                        ).then_inc(msg_ready[g], 16)

            for layer in range(LAYERS):
                if layer:
                    pool.wait_ge(stored, plan.steps * (16 * layer))
                    pool.nop(nofuse=True)
                with pool.Fori(0, plan.rounds) as r:
                    with pool.Fori(0, ITERS - 1) as i:
                        iteration(layer, plan.rounds * layer + r, i)
                    iteration(layer, plan.rounds * layer + r, ITERS - 1)
                    for g in range(RING):
                        pool.wait_ge(msg_ready[g], messages(g))
                    pool.wait_ge(summed, (plan.rounds * layer + r + 1) * GROUPS + RING)
                    pool.nop(nofuse=True)
                    pool.inc_swdge_sem(msg_ready, [messages(g) for g in range(RING)], mode="sub").then_inc(msgs_reset, 1)

        @block.tensor
        def _(pe):
            pe.sem_inc(summed, RING)
            pe.sem_inc(msgs_reset, 1)
            pe.wait_ge(pool_consts, POOL_CONSTS)
            for m in range(2 * BLOCKS):
                at, blk = 1 - m // BLOCKS, m % BLOCKS
                n = P if blk < FULL_BLOCKS else TAIL_UNITS
                pe.wait_ge(rows_float, m // BLOCKS + 1)
                if m >= 2:
                    pe.wait_ge(tr_read, m - 1)
                for j in range(TILES):
                    last = nc.tensor.transpose(
                        ps_tr[m % 2][:, j * P:j * P + n],
                        rows_f[at][0:n, blk, :].rearrange("s (p j) -> s p j", j=TILES)[:, :, j], ident[0:n, 0:n])
                last.then_inc(tr_ready, 1)
            for blk in range(BLOCKS):
                n = P if blk < FULL_BLOCKS else TAIL_UNITS
                pe.wait_ge(diag_ready, blk + 1)
                nc.tensor.matmul(ps_hT[:, blk * P:blk * P + n], ones[0:n, :], diag[0:n, 0:n],
                                 start=True, stop=True).then_inc(plan_psum, 1)
            for n in range(2):
                last = nc.tensor.transpose(ps_inv[0:1, n * P:(n + 1) * P], worst[:, n:n + 1], ident[:])
            last.then_inc(plan_psum, 1)
            for m in range(TURNS):
                t0, t1 = 4 * m, min(4 * m + 4, NODE_TILES)
                pe.wait_ge(pre_h, (t1 - 1) // PT + 1)
                pe.wait_ge(tr_read, 2 * BLOCKS)
                if m >= 2:
                    pe.wait_ge(placed, m - 1)
                for t in range(t0, t1):
                    last = nc.tensor.transpose(ps_tr[m % 2][0:D, (t - t0) * P:(t - t0 + 1) * P], pre_c[:, t, :],
                                               ident[:])
                last.then_inc(turned, 1)
            pe.wait_ge(consts_loaded, 16 * N_CONSTS)
            plan = Plan(pe)

            def iteration(layer, rnd, i, early):
                it = rnd * ITERS + i
                if isinstance(i, int) and i == 0:
                    pe.wait_ge(msgs_reset, rnd + 1)
                    pe.nop(nofuse=True)
                for g in range(RING):
                    n = it * RING + g
                    last_one = isinstance(i, int) and i == ITERS - 1
                    if g == EARLY_AT:
                        early(n)
                    ps = ps_sum[g % 2]
                    pe.wait_ge(onehot_ready, n + rnd + 1)
                    pe.wait_ge(sums_added, 2 * n + 2)
                    pe.wait_ge(msg_ready[g], messages(g) if last_one else 16 * TPG * (i + 1))
                    if layer == 0:
                        pe.wait_ge(attr_ready[g], 16 * UPG * (it + 1))
                    for u in range(UPG):
                        for j in range(TILES if layer == 0 else 0):
                            nc.tensor.matmul(ps[D:P, 1, u, :], ones[:, 0:D], onehot[:, g % 2, u * TILES + j, :],
                                             start=j == 0, stop=j == TILES - 1)
                        for j in range(TILES):
                            t = u * TILES + j
                            if layer == 0:
                                to, what = ps[:, 0, u, :], msg[:, g, t, :]
                            else:
                                to, what = ps[D:P, 0, u, :], msg[:, g, t, D:2 * D]
                            last = nc.tensor.matmul(to, what, onehot[:, g % 2, t, :],
                                                    start=j == 0, stop=j == TILES - 1)
                    last.then_inc(summed, 1)

            def step(layer, tt, here, added):
                cnt = plan.steps * layer + here
                w = wcat[:, layer, :]
                if layer >= 3:
                    edge = plan.steps * (layer - 3) + here
                    pe.wait_ge(inv_ready, cnt + 1)
                    pe.wait_ge(r_ready, edge + 1)
                    pe.nop(nofuse=True)
                    nc.tensor.matmul(ps_inv[0:D, 0:STEP_NODES], ident[D:P, D:P], inv[D:P, :], start=True, stop=True
                                     ).then_inc(inv_low_ready, 1)
                pe.wait_ge(scaled, cnt + 1)
                pe.wait_ge(h_copied, cnt + 1)
                if layer >= 3:
                    pe.wait_ge(r_ready, edge + 2)
                if layer in (0, 1, 3):
                    pe.wait_ge(hT_read, cnt + 1)
                    nc.tensor.matmul(ps_hT[0:D, 0:STEP_NODES], w, zs[:], start=True, stop=layer < 3)
                    if layer >= 3:
                        nc.tensor.matmul(ps_hT[0:D, 0:STEP_NODES], wr[:, layer - 3, :], zr[:], start=False, stop=True)
                pe.wait_ge(node_read, cnt + 1)
                for t in range(STEP_TILES):
                    cols = slice(t * P, (t + 1) * P)
                    last = nc.tensor.matmul(ps_node[:, t, :], zs[:, cols], w, start=True, stop=layer < 3)
                    if layer >= 3:
                        last = nc.tensor.matmul(ps_node[:, t, :], zr[:, cols], wr[:, layer - 3, :],
                                                start=False, stop=True)
                last.then_inc(node_ready, 1)
                if layer == 2:
                    pe.wait_ge(h_ready, cnt + 2)
                    pe.wait_ge(hT_read, cnt + 1)
                    pe.nop(nofuse=True)
                    for t in range(STEP_TILES):
                        last = nc.tensor.transpose(ps_hT[0:D, t * P:(t + 1) * P], hbuf[:, t, :], ident[:])
                    last.then_inc(hT_ready, 1)

            for layer in range(LAYERS):
                loops(pe, plan, layer, iteration, step, peel_last=True)

        @block.vector
        def _(dve):
            dve.sem_inc(sums_added, ADD_CREDIT)
            dve.sem_inc(node_read, 1)
            dve.sem_inc(r_ready, 1)
            once = Serial(dve, dve_serial, 0, 0)
            nc.vector.memset(rows_i[0][0:TAIL_UNITS, FULL_BLOCKS, :], 0)
            nc.vector.memset(rows_i[1][0:TAIL_UNITS, FULL_BLOCKS, :], N)
            nc.vector.memset(pre_x[D:P, NODE_TILES - 1, :], 0.0).then_inc(dve_padded, 1)
            nc.vector.memset(dlow[:], FAR)
            nc.vector.memset(dst_t[:, UNITS * TILES:], FAR)
            once.done(nc.vector.memset(dhigh[:], FAR))

            for k in range(PIECES):
                ts = slice(k * PT, (k + 1) * PT)
                dve.wait_ge(pre_loaded[k], 32 if k == PIECES - 1 else 16)
                once.done(nc.vector.tensor_reduce(pre_mean[:, ts], pre_x[:, ts, :], AX_X, ALU.add))
                once.done(nc.vector.tensor_scalar(pre_mean[:, ts], pre_mean[:, ts], 1.0 / D, None, ALU.mult))
                nc.vector.tensor_tensor(pre_c[:, ts, :], pre_x[:, ts, :],
                                        pre_mean[:, ts].unsqueeze(2).to_broadcast([P, PT, D]), ALU.subtract
                                        ).then_inc(pre_centered, 1)
            dve.wait_ge(rows_float, 1)
            for at, op in ((dlow, ALU.min), (dhigh, ALU.max)):
                nc.vector.tensor_reduce(at[:, 0:FULL_BLOCKS], rows_f[1][:, 0:FULL_BLOCKS, :], AX_X, op)
                ins = nc.vector.tensor_reduce(at[0:TAIL_UNITS, FULL_BLOCKS:BLOCKS],
                                              rows_f[1][0:TAIL_UNITS, FULL_BLOCKS, :], AX_X, op)
            once.done(ins)
            dve.wait_ge(limits_ready, 1)
            nc.vector.tensor_tensor(dspan[:], dhigh[:], dlow[:], ALU.subtract)
            once.done(nc.vector.tensor_tensor(dlate[:], dlate[:], dlow[:], ALU.subtract))
            dve.wait_ge(pool_consts, POOL_CONSTS)
            nc.vector.tensor_reduce(worst[:, 0:1], dspan[:], AX_X, ALU.max)
            nc.vector.tensor_reduce(worst[:, 1:2], dlate[:], AX_X, ALU.max)

            def smallest_dst(blk):
                n = P if blk < FULL_BLOCKS else TAIL_UNITS
                if blk:
                    dve.wait_ge(plan_psum, blk)
                nc.vector.tensor_scalar(diag[0:n, 0:n], ident[0:n, 0:n], dlow[0:n, blk:blk + 1], None,
                                        ALU.mult).then_inc(diag_ready, 1)

            for k in range(PIECES + 1):
                if 0 < k <= BLOCKS:
                    smallest_dst(k - 1)
                if k < PIECES:
                    ts = slice(k * PT, (k + 1) * PT)
                    dve.wait_ge(pre_squared, k + 1)
                    nc.vector.tensor_reduce(pre_var[:, ts], pre_sq[:, ts, :], AX_X, ALU.add).then_inc(pre_summed, 1)
                if k > 0:
                    ts = slice((k - 1) * PT, k * PT)
                    dve.wait_ge(pre_rooted, k)
                    once.done(nc.vector.reciprocal(pre_mean[:, ts], pre_std[:, ts]))
                    nc.vector.tensor_tensor(pre_c[:, ts, :], pre_c[:, ts, :],
                                            pre_mean[:, ts].unsqueeze(2).to_broadcast([P, PT, D]), ALU.mult
                                            ).then_inc(pre_normed, 1)

            dve.wait_ge(plan_psum, BLOCKS + 1)
            dve.wait_ge(tr_read, BLOCKS)
            by_unit = dst_t[:, 0:UNITS * TILES].rearrange("p (s j) -> p s j", j=TILES)
            nc.vector.tensor_tensor(by_unit, by_unit, ps_hT[:, 0:UNITS].unsqueeze(2).to_broadcast([P, UNITS, TILES]),
                                    ALU.subtract)
            nc.vector.tensor_copy(base_f[:], ps_hT[0:1, 0:UNITS])
            once.done(nc.vector.tensor_reduce(worst_row[:], ps_inv[0:1, 0:2 * P].rearrange("o (w p) -> o w p", w=2),
                                              AX_X, ALU.max))
            once.done(nc.vector.tensor_scalar(plan_f[:, 0:1], worst_row[:, 1:2], 0.0, None, ALU.is_le))
            once.done(nc.vector.tensor_scalar(plan_f[:, 1:2], worst_row[:, 0:1], float(WIN), plan_f[:, 0:1],
                                              ALU.is_lt, ALU.mult))
            once.done(nc.vector.tensor_scalar(plan_f[:, 2:3], plan_f[:, 1:2], float(1 - EARLY), float(STEPS),
                                              ALU.mult, ALU.add))
            once.done(nc.vector.tensor_scalar(plan_f[:, 1:2], plan_f[:, 1:2], float(-EARLY), float(STEPS),
                                              ALU.mult, ALU.add))
            nc.vector.tensor_copy(plan_i[:, 0:1], worst_row[:, 0:1])
            nc.vector.tensor_copy(plan_i[:, 1:3], plan_f[:, 1:3]).then_inc(plan_ready, 1)
            plan = Plan(dve)
            for m in range(TURNS):
                c0, c1 = 4 * m * P, min(4 * m + 4, NODE_TILES) * P
                dve.wait_ge(turned, m + 1)
                nc.vector.tensor_copy(z[0][0:D, c0:c1], ps_tr[m % 2][0:D, 0:c1 - c0]).then_inc(placed, 1)
            dve.wait_ge(pre_stored, 16 * PIECES)
            nc.vector.memset(rd[:], 0.0).then_inc(z_cleared, 1)
            dve.wait_ge(z_cleared, 2)
            dve.wait_ge(consts_loaded, 16 * N_CONSTS)

            def where_edges_go(group, half):
                dsts = dst_t[:, bass.ds(TPG * group, TPG)]
                nc.vector.tensor_tensor(
                    onehot[:, half, :, :], dsts.unsqueeze(2).to_broadcast([P, TPG, WIN]),
                    iota_r[:].unsqueeze(1).to_broadcast([P, TPG, WIN]), ALU.is_equal).then_inc(onehot_ready, 1)

            def round_start(layer, rnd):
                nc.vector.tensor_scalar(iota_r[:], iota[:], shift[:, 0:1], None, ALU.add)
                nc.vector.tensor_scalar(base_m[:], base_f[:], shift[0:1, 0:1], float(N), ALU.add, ALU.min
                                        ).then_inc(windows_set, 1)
                dve.wait_ge(windows_set, 2 * rnd + 1)
                nc.vector.tensor_scalar(shift[:], shift[:], float(WIN), None, ALU.add)
                nc.vector.tensor_copy(base_i[:], base_m[:]).then_inc(windows_set, 1)
                dve.wait_ge(windows_set, 2 * rnd + 2)
                dve.nop(nofuse=True)
                where_edges_go(0, 0)

            def iteration(layer, rnd, i, early):
                if isinstance(i, int) and i == 0:
                    round_start(layer, rnd)
                cur = layer % 2
                _, bases = nc.values_load_multi_w_load_instructions(
                    base_i[0:1, bass.ds(RING * UPG * i, RING * UPG)], engines=DVE_ONLY,
                    min_val=0, max_val=N, skip_runtime_bounds_check_because="held at N in round_start")
                for g in range(RING):
                    n = (rnd * ITERS + i) * RING + g
                    if g == EARLY_AT:
                        early(n)
                    where_edges_go(RING * i + (g + 1), (g + 1) % 2)
                    dve.wait_ge(summed, RING + n + 1)
                    for u in range(UPG):
                        dve.wait_ge(sums_added, ADD_CREDIT + 2 * n + u)
                        cols = bass.ds(bases[g * UPG + u], WIN)
                        to = [(z[cur], D, P, 0)]
                        if layer == 0:
                            to += [(rd, D, P, 1), (rd, 0, D, 0)]
                        for buf, lo, hi, kind in to:
                            last = nc.vector.tensor_tensor(buf[lo:hi, cols], buf[lo:hi, cols],
                                                           ps_sum[g % 2][lo:hi, kind, u, :], ALU.add)
                        last.then_inc(sums_added, 1)

            def step(layer, tt, here, added):
                cnt = plan.steps * layer + here
                own = Serial(dve, step_serial[layer], SERIAL[layer], here)
                cols = bass.ds(tt * STEP_NODES, STEP_NODES)
                if layer == 0:
                    dve.wait_ge(sums_added, ADD_CREDIT + 2 * added)
                    dve.nop(nofuse=True)
                own.done(nc.vector.tensor_scalar(inv[D:P, :], rd[D:P, cols], 1.0, None, ALU.max))
                nc.vector.reciprocal(inv[D:P, :], inv[D:P, :]).then_inc(inv_ready, 1)
                dve.wait_ge(inv_ready, cnt + 1)
                if layer > 0:
                    dve.wait_ge(sums_added, ADD_CREDIT + 2 * added)
                    dve.nop(nofuse=True)
                nc.vector.tensor_tensor(zs[D:P, :], z[layer % 2][D:P, cols], inv[D:P, :], ALU.mult).then_inc(scaled, 1)
                if layer >= 3:
                    dve.wait_ge(inv_low_ready, plan.steps * (layer - 3) + here + 1)
                    nc.vector.tensor_tensor(zr[:], rd[0:D, cols], ps_inv[0:D, 0:STEP_NODES], ALU.mult
                                            ).then_inc(r_ready, 1)
                dve.wait_ge(node_ready, cnt + 1)
                dve.wait_ge(h_ready, cnt + 1)
                ins = nc.vector.tensor_tensor(vbuf[:], ps_node[:], bias_bc[:, layer, :].unsqueeze(1)
                                              .to_broadcast([P, STEP_TILES, D]), ALU.add)
                ins.then_inc(node_read, 1)
                if layer == 2:
                    dve.wait_ge(node_read, cnt + 2)
                    dve.wait_ge(x_loaded[2], 16 * (here + 1))
                    nc.vector.tensor_tensor(xs[:], xs[:], vbuf[:], ALU.add).then_inc(x1_ready, 1)
                    dve.wait_ge(x1_ready, here + 1)
                    own.done(nc.vector.tensor_reduce(mean[:], xs[:], AX_X, ALU.add))
                    own.done(nc.vector.tensor_scalar(mean[:], mean[:], 1.0 / D, None, ALU.mult))
                    nc.vector.tensor_tensor(cent[:], xs[:], mean[:].unsqueeze(2).to_broadcast([P, STEP_TILES, D]),
                                            ALU.subtract).then_inc(centered, 1)
                    dve.wait_ge(squared, here + 1)
                    nc.vector.tensor_reduce(var[:], sq[:], AX_X, ALU.add).then_inc(var_ready, 1)
                    dve.wait_ge(std_ready, here + 1)
                    own.done(nc.vector.reciprocal(rstd[:], std[:]))
                    nc.vector.tensor_tensor(cent[:], cent[:], rstd[:].unsqueeze(2).to_broadcast([P, STEP_TILES, D]),
                                            ALU.mult).then_inc(normed, 1)
                elif layer == 4:
                    dve.wait_ge(node_read, cnt + 2)
                    dve.wait_ge(x_loaded[4], 16 * (here + 1))
                    dve.wait_ge(hbuf_free, cnt + 1)
                    nc.vector.scalar_tensor_tensor(out=hbuf[:], in0=vbuf[:], scalar=0.0, in1=xs[:],
                                                   op0=ALU.max, op1=ALU.add).then_inc(h_ready, 1)
                own.end()

            for layer in range(LAYERS):
                once.done(nc.vector.memset(shift[:], 0.0))
                loops(dve, plan, layer, iteration, step)

        @block.scalar
        def _(act):
            act.sem_inc(hT_read, 1)
            act.sem_inc(h_ready, 1)
            act.sem_inc(hbuf_free, 1)
            for k in range(PIECES):
                lo, hi = k * PT, min((k + 1) * PT, NODE_TILES - 1)
                act.dma_start(pre_x[:, lo:hi, :], a["x"][lo * P:hi * P, :].rearrange("(t p) f -> p t f", p=P)
                              ).then_inc(pre_loaded[k], 16)
            act.wait_ge(dve_padded, 1)
            act.dma_start(pre_x[0:LAST_ROWS, NODE_TILES - 1, :], a["x"][N - LAST_ROWS:N, :]
                          ).then_inc(pre_loaded[PIECES - 1], 16)
            act.wait_ge(rows_loaded, 16 * 6)
            for at in (1, 0):
                nc.scalar.copy(rows_f[at][:, 0:FULL_BLOCKS, :], rows_i[at][:, 0:FULL_BLOCKS, :])
                nc.scalar.copy(rows_f[at][0:TAIL_UNITS, FULL_BLOCKS, :], rows_i[at][0:TAIL_UNITS, FULL_BLOCKS, :]
                               ).then_inc(rows_float, 1)
            act.wait_ge(pool_consts, POOL_CONSTS)

            def square(k):
                ts = slice(k * PT, (k + 1) * PT)
                act.wait_ge(pre_centered, k + 1)
                nc.scalar.activation(pre_sq[:, ts, :], pre_c[:, ts, :], ACT.Square).then_inc(pre_squared, 1)

            def list_block(m):
                at, blk = 1 - m // BLOCKS, m % BLOCKS
                n = P if blk < FULL_BLOCKS else TAIL_UNITS
                to = dst_t if at else src_t
                act.wait_ge(tr_ready, m + 1)
                nc.scalar.copy(to[:, blk * UNIT:blk * UNIT + n * TILES].rearrange("p (s j) -> p j s", j=TILES),
                               ps_tr[m % 2][:].rearrange("p (j s) -> p j s", j=TILES)[:, :, 0:n]).then_inc(tr_read, 1)

            for k in range(PIECES):
                square(k)
                list_block(k)
            list_block(PIECES)
            for k in range(PIECES + 1):
                if k < PIECES:
                    ts = slice(k * PT, (k + 1) * PT)
                    act.wait_ge(pre_summed, k + 1)
                    nc.scalar.activation(pre_std[:, ts], pre_var[:, ts], ACT.Sqrt, bias=eps[:, 0:1], scale=1.0 / D
                                         ).then_inc(pre_rooted, 1)
                if k > 0:
                    ts = slice((k - 1) * PT, k * PT)
                    act.wait_ge(pre_normed, k)
                    nc.scalar.activation(pre_c[:, ts, :], pre_c[:, ts, :], ACT.Relu).then_inc(pre_h, 1)
            plan = Plan(act)

            def iteration(layer, rnd, i, early):
                it = rnd * ITERS + i
                for g in range(RING):
                    if g == EARLY_AT:
                        early(None)
                    act.wait_ge(summed, it * RING + g + 1)
                    nc.scalar.copy(idx[:, g, :], src_t[:, bass.ds(RING * TPG * i + TPG * g, TPG)]
                                   ).then_inc(idx_ready, 1)
                if layer < LAYERS - 1:
                    nc.scalar.copy(z[(layer + 1) % 2][D:P, bass.ds(ZPIECE * i, ZPIECE)], zeros[D:P, :])

            def step(layer, tt, here, added):
                cnt = plan.steps * layer + here
                cur, nxt = layer % 2, (layer + 1) % 2
                cols = bass.ds(tt * STEP_NODES, STEP_NODES)
                act.wait_ge(node_read, cnt + 1)
                if layer == 0:
                    act.wait_ge(placed, TURNS)
                nc.scalar.copy(zs[0:D, :], z[cur][0:D, cols]).then_inc(h_copied, 1)
                if layer in (0, 1, 3):
                    act.wait_ge(node_read, cnt + 2)
                    act.wait_ge(hbuf_free, cnt + 1)
                    nc.scalar.activation(hbuf[:], vbuf[:], ACT.Relu).then_inc(h_ready, 1)
                    nc.scalar.activation(z[nxt][0:D, cols], ps_hT[0:D, 0:STEP_NODES], ACT.Relu,
                                         bias=bias_col[:, layer:layer + 1]).then_inc(hT_read, 1)
                elif layer == 2:
                    act.wait_ge(centered, here + 1)
                    nc.scalar.activation(sq[:], cent[:], ACT.Square).then_inc(squared, 1)
                    act.wait_ge(var_ready, here + 1)
                    nc.scalar.activation(std[:], var[:], ACT.Sqrt, bias=eps[:, 0:1], scale=1.0 / D
                                         ).then_inc(std_ready, 1)
                    act.wait_ge(normed, here + 1)
                    act.wait_ge(hbuf_free, cnt + 1)
                    nc.scalar.activation(hbuf[:], cent[:], ACT.Relu).then_inc(h_ready, 1)
                    act.wait_ge(hT_ready, here + 1)
                    nc.scalar.copy(z[nxt][0:D, cols], ps_hT[0:D, 0:STEP_NODES]).then_inc(hT_read, 1)

            for layer in range(LAYERS):
                loops(act, plan, layer, iteration, step, behind=1)


_INS = ["x", "src", "dst", "edge_attr_64", "L0_gnn_w_self1", "L0_gnn_w_nei1", "L0_gnn_b1", "L0_gnn_w_self2",
        "L0_gnn_w_nei2", "L0_gnn_b2", "L0_gnn_w_self3", "L0_gnn_w_nei3", "L0_gnn_b3", "L1_gnn_W1", "L1_gnn_b1",
        "L1_gnn_W2", "L1_gnn_b2"]


def kernel(**inputs):
    import numpy as np
    import concourse.bacc as bacc
    from concourse.bass_utils import run_bass_kernel_spmd

    nc = bacc.Bacc("TRN2", target_bir_lowering=False, num_devices=1)
    arrays, aps = {}, {}
    for name in _INS:
        v = np.ascontiguousarray(inputs[name])
        arrays[f"in_{name}"] = v
        aps[name] = nc.dram_tensor(f"in_{name}", v.shape, mybir.dt.from_np(v.dtype), kind="ExternalInput").ap()
    out = nc.dram_tensor("out_0", (N, D), F32, kind="ExternalOutput").ap()
    program(nc, aps, out)
    r = run_bass_kernel_spmd(nc, [arrays], core_ids=[0])
    return r.results[0]["out_0"]
```
